# Optimizing a Trainium2 kernel written in Bass

```python
import numpy as np
import jax
import jax.numpy as jnp

def _softmax(x, axis=-1):
    return jax.nn.softmax(x, axis=axis)

def _gelu(x):
    return jax.nn.gelu(x, approximate=True)

def _silu(x):
    return jax.nn.silu(x)

def _sigmoid(x):
    return jax.nn.sigmoid(x)

def _layernorm(x, axis=-1, eps=1e-05):
    m = jnp.mean(x, axis=axis, keepdims=True)
    v = jnp.var(x, axis=axis, keepdims=True)
    return (x - m) / jnp.sqrt(v + eps)

def _scatter_add(tgt, idx, src, axis=0):
    return tgt.at[idx].add(src)

def _segment_sum(src, seg, n):
    return jax.ops.segment_sum(src, seg, n)
kernel_name = 'mk_flamingo_gated_d1_seqx_r8_b203c1'

def setup_inputs(seed: int=0):
    np.random.seed(seed)
    _w = jnp.asarray

    def _rec_inputs():
        import jax
        import jax.numpy as jnp
        _rk = jax.random.key(seed)
        x = -0.0005207 + 1.001 * jax.random.normal(jax.random.fold_in(_rk, 1), (8, 128, 256), jnp.float32)
        _lenS = 128 - jax.random.randint(jax.random.fold_in(_rk, 7), (8,), 0, max(1, 128 // 4) + 1, jnp.int32)
        _lenS2 = 128 - jax.random.randint(jax.random.fold_in(_rk, 8), (8,), 0, max(1, 128 // 4) + 1, jnp.int32)
        _ctx_2048P = jax.random.normal(jax.random.fold_in(_rk, 11), (8, 16, 256), jnp.float32)
        _ctx_2048c = jax.random.dirichlet(jax.random.fold_in(_rk, 511), 0.3 * jnp.ones((16,), jnp.float32), (8, 128))
        _ctx_2048t = jnp.einsum('bsk,bkd->bsd', _ctx_2048c, _ctx_2048P)
        _ctx_2048t = _ctx_2048t * jax.lax.rsqrt(jnp.mean(jnp.square(_ctx_2048t)) + 1e-12) * 0.953939
        ctx_2048 = -0.000514642 + 1.00011 * (_ctx_2048t + 0.3 * jax.random.normal(jax.random.fold_in(_rk, 611), (8, 128, 256), jnp.float32))
        _g = jax.random.normal(jax.random.fold_in(_rk, 9001), (2, 1), jnp.float32)
        _g = jnp.sign(_g) * jnp.maximum(jnp.abs(_g), 1.0) + (_g == 0) * 1.0
        g_xattn = _g[0]
        g_ffn = _g[1]
        return (x, ctx_2048, g_xattn, g_ffn)
    x, ctx_2048, g_xattn, g_ffn = _rec_inputs()

    def _L0_xattn_setup():
        import jax, jax.numpy as jnp
        import numpy as np
        from math import sqrt
        key = jax.random.key(seed)
        kq, kk, kv = jax.random.split(key, 3)
        B, D, N = (8, 128, 256)
        Q = jax.random.normal(kq, (B, D, N), dtype=jnp.float32)
        K = jax.random.normal(kk, (B, D, N), dtype=jnp.float32)
        V = jax.random.normal(kv, (B, D, N), dtype=jnp.float32)
        return {'Q': Q, 'K': K, 'V': V}
    _L0_xattn_all = _L0_xattn_setup()
    _L0_xattn_in = {k: v for k, v in _L0_xattn_all.items() if k in ()}
    del _L0_xattn_all

    def _L0_ffn_setup():
        import jax, jax.numpy as jnp
        import numpy as np
        EPS = 1e-08

        def _bit_quant(w):
            scale = jnp.maximum(jnp.mean(jnp.abs(w)), EPS)
            w_ternary = jnp.clip(jnp.round(w / scale), -1.0, 1.0)
            return w + jax.lax.stop_gradient(w_ternary - w)
        key = jax.random.key(seed)
        k = jax.random.split(key, 5)
        emb, dff = (256, 1024)
        B, S = (4, 256)
        x = jax.random.normal(k[0], (B, S, emb), dtype=jnp.float32)
        w1 = jax.random.normal(k[1], (dff, emb), dtype=jnp.float32) * 0.02
        b1 = jax.random.normal(k[2], (dff,), dtype=jnp.float32) * 0.02
        w2 = jax.random.normal(k[3], (emb, dff), dtype=jnp.float32) * 0.02
        b2 = jax.random.normal(k[4], (emb,), dtype=jnp.float32) * 0.02
        return {'x': x, 'w1': w1, 'b1': b1, 'w2': w2, 'b2': b2}
    _L0_ffn_all = _L0_ffn_setup()
    _L0_ffn_in = {k: v for k, v in _L0_ffn_all.items() if k in ('w1', 'b1', 'w2', 'b2')}
    del _L0_ffn_all
    return {'x': x, 'ctx_2048': ctx_2048, 'g_xattn': g_xattn, 'g_ffn': g_ffn, 'L0_ffn_w1': _L0_ffn_in['w1'], 'L0_ffn_b1': _L0_ffn_in['b1'], 'L0_ffn_w2': _L0_ffn_in['w2'], 'L0_ffn_b2': _L0_ffn_in['b2']}

def reference(x, ctx_2048, g_xattn, g_ffn, L0_ffn_w1, L0_ffn_b1, L0_ffn_w2, L0_ffn_b2):
    import jax
    import jax.numpy as jnp

    def _L0_xattn_ref(Q, K, V):
        import jax, jax.numpy as jnp
        import numpy as np
        from math import sqrt
        dk = Q.shape[1]
        x = jnp.einsum('bdn,bdm->bnm', Q, K) / sqrt(dk)
        score = jax.nn.sigmoid(x)
        out = jnp.einsum('bvn,bnm->bvm', V, score)
        return out

    def _L0_ffn_ref(x, w1, b1, w2, b2):
        import jax, jax.numpy as jnp
        import numpy as np
        EPS = 1e-08

        def _bit_quant(w):
            scale = jnp.maximum(jnp.mean(jnp.abs(w)), EPS)
            w_ternary = jnp.clip(jnp.round(w / scale), -1.0, 1.0)
            return w + jax.lax.stop_gradient(w_ternary - w)
        w1q = _bit_quant(w1)
        w2q = _bit_quant(w2)
        h = jnp.einsum('bsd,fd->bsf', x, w1q) + b1
        h = jax.nn.gelu(h, approximate=False)
        return jnp.einsum('bsf,df->bsd', h, w2q) + b2
    x = x + jnp.tanh(g_xattn[0]) * _L0_xattn_ref(_layernorm(x, axis=-1), ctx_2048, ctx_2048)
    x = x + jnp.tanh(g_ffn[0]) * _L0_ffn_ref(_layernorm(x, axis=-1), L0_ffn_w1, L0_ffn_b1, L0_ffn_w2, L0_ffn_b2)
    return x

_drawn_inputs = setup_inputs


def setup_inputs(seed=0):
    import zlib

    import numpy as np

    out = dict(_drawn_inputs(seed))
    spreads = {}
    factors = {'L0_ffn_b1': 38.022, 'L0_ffn_b2': 64.0}
    for name, (base, spread) in spreads.items():
        noise = np.random.default_rng([zlib.crc32(name.encode()), seed]).standard_normal(out[name].shape)
        drawn = base * np.exp(spread * noise) if base else spread * noise
        out[name] = jnp.asarray(drawn.astype(out[name].dtype))
    for name, factor in factors.items():
        out[name] = (out[name] * factor).astype(out[name].dtype)
    return out
```

```python
from contextlib import ExitStack

import concourse.bass as bass
from concourse import mybir

F32 = mybir.dt.float32
F32R = mybir.dt.float32r
BF16 = mybir.dt.bfloat16
ALU = mybir.AluOpType
ACT = mybir.ActivationFunctionType

P = 128


def flamingo_gated_block(
    nc: bass.Bass,
    x: bass.AP,
    ctx_kv: bass.AP,
    g_xattn: bass.AP,
    g_ffn: bass.AP,
    w1: bass.AP,
    b1: bass.AP,
    w2: bass.AP,
    b2: bass.AP,
    out: bass.AP,
):
    B, D, N = x.shape
    F = w1.shape[0]
    NC = N // P
    FC = F // P
    TOKENS = B * D
    PAIRS = B // 2
    GROUP = 512
    NG = TOKENS // GROUP
    BPG = GROUP // D
    HALF_W = FC // 2
    SM_SCALE = float(D) ** -0.5
    LN_EPS = 1e-5
    QUANT_EPS = 1e-8
    HALF_MEAN = 0.5 / (F * N)
    assert D == P and N == 2 * P and F % (2 * P) == 0 and TOKENS % GROUP == 0

    with ExitStack() as stack:
        def sb(name, shape, dt=F32):
            return stack.enter_context(nc.sbuf_tensor(name, shape, dt))

        def sem(name):
            return stack.enter_context(nc.semaphore(name))

        x_sb = sb("x_sb", [P, B, N])
        c_sb = sb("c_sb", [P, B, N])
        w1_sb = sb("w1_sb", [P, FC, N])
        w2_sb = sb("w2_sb", [P, NC, F])
        b1_sb = sb("b1_sb", [P, FC])
        b2_sb = sb("b2_sb", [P, N])
        gates = sb("gates", [P, 2])
        ident = sb("ident", [P, P])
        ident16 = sb("ident16", [P, P], BF16)
        ones = sb("ones", [P, P])
        neg_half = sb("neg_half", [P, B])
        stats1 = sb("stats1", [P, B, 6])
        mv1 = sb("mv1", [P, B, 2])
        var1 = sb("var1", [P, B])
        rstd1 = sb("rstd1", [P, B])
        q_sb = sb("q_sb", [P, B, N])
        ctxT = sb("ctxT", [P, B, NC, P])
        PR = 3
        probs = sb("probs", [P, PR, NC, N])
        tg = sb("tg", [P, 2])
        x1 = sb("x1", [P, B, N])
        stats2 = sb("stats2", [P, B, 6])
        mv2 = sb("mv2", [P, B, 2])
        var2 = sb("var2", [P, B])
        rstd2 = sb("rstd2", [P, B])
        z_sb = sb("z_sb", [P, B, N])
        zT_hi = sb("zT_hi", [P, NC, TOKENS], F32R)
        zT_lo = sb("zT_lo", [P, NC, TOKENS], F32R)
        w_abs = sb("w_abs", [P, F * N // P], BF16)
        row_abs = sb("row_abs", [P, 2])
        thr = sb("thr", [P, 2])
        neg_thr = sb("neg_thr", [P, 2])
        below = sb("below", [P, F * N // P], BF16)
        t1 = sb("t1", [P, FC, N], BF16)
        t2 = sb("t2", [P, NC, F], BF16)
        w1T = sb("w1T", [P, NC, FC, P], F32R)
        w2T = sb("w2T", [P, FC, N], F32R)
        GR = 3
        act = sb("act", [P, GR, GROUP])
        act_hi = sb("act_hi", [P, NG, FC, GROUP], F32R)
        act_lo = sb("act_lo", [P, NG, FC, GROUP], F32R)
        b2g = sb("b2g", [P, N])
        x1b = sb("x1b", [P, B, N])
        out_sb = q_sb

        banks = [stack.enter_context(nc.psum_tensor(f"bank{i}", [P, 512], F32)) for i in range(8)]
        score_ps = [banks[0], banks[1]]
        pv_ps = [banks[2], banks[3]]
        tr_ps = [banks[4], banks[5]]
        z_ps = [banks[6], banks[7], banks[6], banks[4]]
        mean_ps = banks[7]
        wt_ps = [banks[4], banks[5], banks[5], banks[4]]
        h_ps = [banks[0], banks[1], banks[6], banks[7]]
        NH = len(h_ps)
        o_ps = [banks[2], banks[3]]

        x_loads = [(0, 1), (1, 2), (2, 4), (4, 8)]
        load_of = [next(i for i, (a, b) in enumerate(x_loads) if a <= n < b) for n in range(B)]
        x_in = [sem(f"x_in{i}") for i in range(len(x_loads))]
        c_in = [sem(f"c_in{i}") for i in range(len(x_loads))]
        w1_in, w2_in = sem("w1_in"), sem("w2_in")
        g1_in, g2_in, b1_in, b2_in = sem("g1_in"), sem("g2_in"), sem("b1_in"), sem("b2_in")
        ident_zero, ident_one, ident_ready, const_ready = (
            sem("ident_zero"), sem("ident_one"), sem("ident_ready"), sem("const_ready"))
        stats1_done, mv1_done, var1_done, rstd1_done, q_done = (
            sem("stats1_done"), sem("mv1_done"), sem("var1_done"), sem("rstd1_done"), sem("q_done"))
        ctx_tr, ctxT_done = sem("ctx_tr"), sem("ctxT_done")
        scores_done, probs_done, pv_done = sem("scores_done"), sem("probs_done"), sem("pv_done")
        tg_done, x1_done = sem("tg_done"), sem("x1_done")
        stats2_done, mv2_done, var2_done, rstd2_done, z_done = (
            sem("stats2_done"), sem("mv2_done"), sem("var2_done"), sem("rstd2_done"), sem("z_done"))
        z_tr, zhi_done, zlo_done = sem("z_tr"), sem("zhi_done"), sem("zlo_done")
        abs_done, mean_done, thr_done = sem("abs_done"), sem("mean_done"), sem("thr_done")
        below_done, tern_done = sem("below_done"), sem("tern_done")
        w_tr, wT_done = sem("w_tr"), sem("wT_done")
        h_done, act_done, hi_done, lo_done = sem("h_done"), sem("act_done"), sem("hi_done"), sem("lo_done")
        b2g_done, x1b_done, o_done, out_done, stored = (
            sem("b2g_done"), sem("x1b_done"), sem("o_done"), sem("out_done"), sem("stored"))

        x_dram = x.rearrange("b d n -> d b n")
        c_dram = ctx_kv.rearrange("b d n -> d b n")
        out_dram = out.rearrange("b d n -> d b n")
        w1_dram = w1.rearrange("(p j) n -> p j n", j=FC)
        b1_dram = b1.rearrange("(p j) -> p j", j=FC)
        w2_dram = w2.rearrange("(c p) f -> p c f", p=P)

        block = stack.enter_context(nc.Block())

        @block.sync
        def _(sp):
            for i, (a, b) in enumerate(x_loads):
                sp.dma_start(x_sb[:, a:b, :], x_dram[:, a:b, :]).then_inc(x_in[i], 16)
                sp.dma_start(c_sb[:, a:b, :], c_dram[:, a:b, :]).then_inc(c_in[i], 16)
            sp.dma_start(w1_sb[:, :, :], w1_dram).then_inc(w1_in, 16)
            sp.dma_start(w2_sb[:, :, :], w2_dram).then_inc(w2_in, 16)
            for b in range(B):
                sp.wait_ge(out_done, b + 1)
                sp.dma_start(out_dram[:, b, :], out_sb[:, b, :]).then_inc(stored, 16)
            sp.wait_ge(stored, 16 * B)

        @block.gpsimd
        def _(pool):
            pool.dma_start(gates[:, 0:1], g_xattn.partition_broadcast(P)).then_inc(g1_in, 16)
            nc.gpsimd.memset(ident[:, :], 0.0).then_inc(ident_zero, 1)
            nc.gpsimd.memset(neg_half[:, :], -0.5).then_inc(const_ready, 1)
            pool.wait_ge(ident_zero, 1)
            nc.gpsimd.affine_select(out=ident[:, :], in_=ident[:, :], compare_op=ALU.not_equal, fill=1.0,
                                    base=0, pattern=[[-1, P]], channel_multiplier=1).then_inc(ident_one, 1)

            def rstd(mv, var, r, mv_sem, var_sem, r_sem, a, b):
                pool.wait_ge(mv_sem, b)
                nc.gpsimd.tensor_scalar(var[:, a:b], mv[:, a:b, 1], LN_EPS, None, ALU.add).then_inc(var_sem, b - a)
                pool.wait_ge(var_sem, b)
                pool.wait_ge(const_ready, 1)
                nc.gpsimd.tensor_tensor(r[:, a:b], var[:, a:b], neg_half[:, a:b], ALU.pow).then_inc(r_sem, b - a)

            rstd(mv1, var1, rstd1, mv1_done, var1_done, rstd1_done, 0, 1)
            pool.dma_start(gates[:, 1:2], g_ffn.partition_broadcast(P)).then_inc(g2_in, 16)
            pool.dma_start(b1_sb[:, :], b1_dram).then_inc(b1_in, 16)
            pool.dma_start(b2_sb[:, :], b2.partition_broadcast(P)).then_inc(b2_in, 16)
            rstd(mv1, var1, rstd1, mv1_done, var1_done, rstd1_done, 1, 2)
            rstd(mv1, var1, rstd1, mv1_done, var1_done, rstd1_done, 2, 4)
            for b in range(B):
                rstd(mv2, var2, rstd2, mv2_done, var2_done, rstd2_done, b, b + 1)
                if b in (0, 2):
                    rstd(mv1, var1, rstd1, mv1_done, var1_done, rstd1_done, b + 4, b + 6)
            pool.wait_ge(b2_in, 16)
            pool.wait_ge(tg_done, 1)
            nc.gpsimd.tensor_scalar(b2g[:, :], b2_sb[:, :], tg[:, 1:2], 1.0, ALU.mult, ALU.mult).then_inc(b2g_done, 1)
            pool.wait_ge(b2g_done, 1)
            for b in range(B):
                pool.wait_ge(x1_done, b + 1)
                nc.gpsimd.tensor_tensor(x1b[:, b, :], x1[:, b, :], b2g[:, :], ALU.add).then_inc(x1b_done, 1)

        @block.scalar
        def _(act_e):
            nc.scalar.preload_act_table(ACT.Sigmoid)

            def ctxT_copy(b):
                act_e.wait_ge(ctx_tr, b + 1)
                nc.scalar.activation(ctxT[:, b, :, :], tr_ps[b % 2][:, 0:N].rearrange("p (c v) -> p c v", c=NC),
                                     ACT.Copy).then_inc(ctxT_done, 1)

            def sigmoid(b):
                act_e.wait_ge(scores_done, b + 1)
                if b >= PR:
                    act_e.wait_ge(pv_done, b - PR + 1)
                nc.scalar.activation(probs[:, b % PR, :, :], score_ps[b % 2][:, :].rearrange("p (c m) -> p c m", c=NC),
                                     ACT.Sigmoid, scale=SM_SCALE).then_inc(probs_done, 1)

            def z_hi(k):
                act_e.wait_ge(z_tr, k + 1)
                nc.scalar.activation(
                    zT_hi[:, :, 2 * k * P:(2 * k + 2) * P].rearrange("p c (b t) -> p b c t", b=2),
                    z_ps[k][:, :].rearrange("p (b c t) -> p b c t", b=2, c=NC), ACT.Copy).then_inc(zhi_done, 1)

            def abs_sum(w, i, w_sem):
                act_e.wait_ge(w_sem, 16)
                if i:
                    act_e.wait_ge(abs_done, i)
                nc.scalar.activation(w_abs[:, :], w, ACT.Abs, accum_out=row_abs[:, i:i + 1]).then_inc(abs_done, 1)

            def wT_copy(dst, i):
                act_e.wait_ge(w_tr, i + 1)
                nc.scalar.activation(dst, wt_ps[i][:, :].bitcast(BF16), ACT.Copy).then_inc(wT_done, 1)

            def gelu(u):
                g, j = divmod(u, FC)
                act_e.wait_ge(h_done, u + 1)
                if u == 0:
                    act_e.wait_ge(b1_in, 16)
                if u >= GR:
                    act_e.wait_ge(lo_done, u - GR + 1)
                nc.scalar.activation(act[:, u % GR, :], h_ps[u % NH][:, :], ACT.Gelu,
                                     bias=b1_sb[:, j:j + 1]).then_inc(act_done, 1)
                nc.scalar.activation(act_hi[:, g, j, :], h_ps[u % NH][:, :], ACT.Gelu,
                                     bias=b1_sb[:, j:j + 1]).then_inc(hi_done, 1)

            ctxT_copy(0)
            sigmoid(0)
            act_e.wait_ge(g1_in, 16)
            act_e.wait_ge(g2_in, 16)
            nc.scalar.activation(tg[:, :], gates[:, :], ACT.Tanh).then_inc(tg_done, 1)
            for b in range(1, B):
                ctxT_copy(b)
                sigmoid(b)
                if b == 4:
                    abs_sum(w1_sb[:, :, :].rearrange("p j n -> p (j n)"), 0, w1_in)
                if b == 3:
                    z_hi(0)
                if b == 5:
                    z_hi(1)
                if b == 6:
                    abs_sum(w2_sb[:, :, :].rearrange("p c f -> p (c f)"), 1, w2_in)
                if b == 7:
                    for c in range(NC):
                        wT_copy(w1T[:, c, :, :].rearrange("p j f -> p (j f)"), c)
            z_hi(2)
            z_hi(3)
            for u in range(NG * FC):
                gelu(u)
                if u == FC - 1:
                    for h in range(2):
                        wT_copy(w2T[:, h * HALF_W:(h + 1) * HALF_W, :].rearrange("p j d -> p (j d)"), 2 + h)

        @block.vector
        def _(dve):
            nc.vector.memset(ones[:, :], 1.0).then_inc(const_ready, 1)
            dve.wait_ge(ident_one, 1)
            nc.vector.tensor_copy(ident16[:, :], ident[:, :]).then_inc(ident_ready, 1)

            def ln_stats(src, stats, mv, s_sem, mv_sem, b):
                nc.vector.bn_stats(stats[:, b, :], src[:, b, :]).then_inc(s_sem, 1)
                dve.wait_ge(s_sem, b + 1)
                nc.vector.bn_aggr(mv[:, b, :], stats[:, b, :]).then_inc(mv_sem, 1)

            def stats_x(b):
                dve.wait_ge(x_in[load_of[b]], 16)
                ln_stats(x_sb, stats1, mv1, stats1_done, mv1_done, b)

            def normed(dst, src, mv, r, r_sem, d_sem, b):
                dve.wait_ge(r_sem, b + 1)
                nc.vector.tensor_scalar(dst[:, b, :], src[:, b, :], mv[:, b, 0:1], r[:, b:b + 1],
                                        ALU.subtract, ALU.mult).then_inc(d_sem, 1)

            def q_of(b):
                normed(q_sb, x_sb, mv1, rstd1, rstd1_done, q_done, b)

            def residual1(b):
                dve.wait_ge(pv_done, b + 1)
                dve.wait_ge(tg_done, 1)
                nc.vector.scalar_tensor_tensor(out=x1[:, b, :], in0=pv_ps[b % 2][:, 0:N], scalar=tg[:, 0:1],
                                               in1=x_sb[:, b, :], op0=ALU.mult, op1=ALU.add).then_inc(x1_done, 1)
                dve.wait_ge(x1_done, b + 1)
                ln_stats(x1, stats2, mv2, stats2_done, mv2_done, b)

            def z_of(b):
                normed(z_sb, x1, mv2, rstd2, rstd2_done, z_done, b)

            def z_lo(k):
                dve.wait_ge(zhi_done, k + 1)
                tokens = slice(2 * k * P, (2 * k + 2) * P)
                nc.vector.tensor_tensor(
                    zT_lo[:, :, tokens].rearrange("p c (b t) -> p b c t", b=2),
                    z_ps[k][:, :].rearrange("p (b c t) -> p b c t", b=2, c=NC),
                    zT_hi[:, :, tokens].bitcast(F32).rearrange("p c (b t) -> p b c t", b=2),
                    ALU.subtract).then_inc(zlo_done, 1)

            def threshold(i):
                dve.wait_ge(mean_done, i + 1)
                nc.vector.tensor_scalar(thr[:, i:i + 1], mean_ps[:, 0:1], HALF_MEAN, 0.5 * QUANT_EPS,
                                        ALU.mult, ALU.max).then_inc(thr_done, 1)
                nc.vector.tensor_scalar(neg_thr[:, i:i + 1], mean_ps[:, 0:1], -HALF_MEAN, -0.5 * QUANT_EPS,
                                        ALU.mult, ALU.min).then_inc(thr_done, 1)

            def ternary(w, t, i, h, n):
                step = F * N // P // n
                part = slice(h * step, (h + 1) * step)
                dve.wait_ge(thr_done, 2 * i + 2)
                nc.vector.tensor_scalar(below[:, part], w[:, part], neg_thr[:, i:i + 1], None,
                                        ALU.is_lt).then_inc(below_done, 1)
                dve.wait_ge(below_done, i * n + h + 1)
                nc.vector.scalar_tensor_tensor(out=t[:, part], in0=w[:, part], scalar=thr[:, i:i + 1],
                                               in1=below[:, part], op0=ALU.is_gt,
                                               op1=ALU.subtract).then_inc(tern_done, 1)

            def ternary1(h):
                ternary(w1_sb[:, :, :].rearrange("p j n -> p (j n)"), t1[:, :, :].rearrange("p j n -> p (j n)"), 0, h, 2)

            def ternary2(h):
                if h == 0:
                    dve.wait_ge(tern_done, 2)
                ternary(w2_sb[:, :, :].rearrange("p c f -> p (c f)"), t2[:, :, :].rearrange("p c f -> p (c f)"), 1, h, 2)

            def act_rest(u):
                g, j = divmod(u, FC)
                dve.wait_ge(act_done, u + 1)
                dve.wait_ge(hi_done, u + 1)
                nc.vector.tensor_tensor(act_lo[:, g, j, :], act[:, u % GR, :], act_hi[:, g, j, :].bitcast(F32),
                                        ALU.subtract).then_inc(lo_done, 1)

            def residual2(b):
                dve.wait_ge(o_done, b + 1)
                dve.wait_ge(x1b_done, b + 1)
                nc.vector.scalar_tensor_tensor(out=out_sb[:, b, :], in0=o_ps[b % 2][:, 0:N], scalar=tg[:, 1:2],
                                               in1=x1b[:, b, :], op0=ALU.mult, op1=ALU.add).then_inc(out_done, 1)

            stats_x(0)
            stats_x(1)
            q_of(0)
            stats_x(2)
            q_of(1)
            stats_x(3)
            for b in range(B):
                if b + 4 < B:
                    stats_x(b + 4)
                if b + 2 < B:
                    q_of(b + 2)
                residual1(b)
                if b >= 1:
                    z_of(b - 1)
                if b == 3:
                    z_lo(0)
                if b == 5:
                    threshold(0)
                    z_lo(1)
                    ternary1(0)
                if b == 6:
                    ternary1(1)
                if b == 7:
                    threshold(1)
            z_of(B - 1)
            z_lo(2)
            z_lo(3)
            ternary2(0)
            ternary2(1)
            for u in range(NG * FC):
                act_rest(u)
                if u >= 2 * FC - 2:
                    pass
            for b in range(B):
                residual2(b)

        @block.tensor
        def _(pe):
            def ctx_transposes(b):
                pe.wait_ge(c_in[load_of[b]], 16)
                if b >= 2:
                    pe.wait_ge(ctxT_done, b - 1)
                for c in range(NC):
                    mm = nc.tensor.transpose(tr_ps[b % 2][:, c * P:(c + 1) * P], c_sb[:, b, c * P:(c + 1) * P],
                                             ident[:, :])
                mm.then_inc(ctx_tr, 1)

            def scores(b):
                pe.wait_ge(q_done, b + 1)
                if b >= 2:
                    pe.wait_ge(probs_done, b - 1)
                for c in range(NC):
                    mm = nc.tensor.matmul(score_ps[b % 2][:, c * N:(c + 1) * N], q_sb[:, b, c * P:(c + 1) * P],
                                          c_sb[:, b, :], start=True, stop=True)
                mm.then_inc(scores_done, 1)

            def pv(b):
                pe.wait_ge(ctxT_done, b + 1)
                pe.wait_ge(probs_done, b + 1)
                if b >= 2:
                    pe.wait_ge(x1_done, b - 1)
                for c in range(NC):
                    mm = nc.tensor.matmul(pv_ps[b % 2][:, 0:N], ctxT[:, b, c, :], probs[:, b % PR, c, :],
                                          start=(c == 0), stop=(c == NC - 1))
                mm.then_inc(pv_done, 1)

            def z_transposes(k):
                pe.wait_ge(z_done, 2 * k + 2)
                if k == 1:
                    pe.wait_ge(thr_done, 2)
                if k == 2:
                    pe.wait_ge(zlo_done, 1)
                if k == 3:
                    pe.wait_ge(wT_done, 1)
                for b in range(2):
                    for c in range(NC):
                        mm = nc.tensor.transpose(z_ps[k][:, (2 * b + c) * P:(2 * b + c + 1) * P],
                                                 z_sb[:, 2 * k + b, c * P:(c + 1) * P], ident[:, :])
                mm.then_inc(z_tr, 1)

            def mean(i):
                pe.wait_ge(abs_done, i + 1)
                pe.wait_ge(const_ready, 2)
                if i == 1:
                    pe.wait_ge(zlo_done, 2)
                nc.tensor.matmul(mean_ps[:, 0:1], ones[:, :], row_abs[:, i:i + 1], start=True,
                                 stop=True).then_inc(mean_done, 1)

            def w1_transposes():
                pe.wait_ge(tern_done, 2)
                pe.wait_ge(ctxT_done, B)
                for c in range(NC):
                    for j in range(FC):
                        mm = nc.tensor.transpose(wt_ps[c][:, :].bitcast(BF16)[:, j * P:(j + 1) * P],
                                                 t1[:, j, c * P:(c + 1) * P], ident16[:, :])
                    mm.then_inc(w_tr, 1)

            def w2_transposes(h):
                pe.wait_ge(tern_done, 4)
                pe.wait_ge(wT_done, 2)
                if h == 1:
                    pe.wait_ge(zlo_done, 4)
                by_slot = t2[:, :, :].rearrange("p c (f j) -> p c j f", j=FC)
                for j in range(HALF_W):
                    for c in range(NC):
                        mm = nc.tensor.transpose(
                            wt_ps[2 + h][:, :].bitcast(BF16)[:, (j * NC + c) * P:(j * NC + c + 1) * P],
                            by_slot[:, c, h * HALF_W + j, :], ident16[:, :])
                mm.then_inc(w_tr, 1)

            def up(u):
                g, j = divmod(u, FC)
                if j == 0:
                    pe.wait_ge(zlo_done, (g + 1) * BPG // 2)
                if u == 0:
                    pe.wait_ge(wT_done, 2)
                if u >= NH:
                    pe.wait_ge(hi_done, u - NH + 1)
                elif u < 2:
                    pe.wait_ge(probs_done, B)
                elif u == 2:
                    pe.wait_ge(zlo_done, 3)
                else:
                    pe.wait_ge(thr_done, 4)
                tokens = slice(g * GROUP, (g + 1) * GROUP)
                for c in range(NC):
                    for k, part in enumerate((zT_hi, zT_lo)):
                        mm = nc.tensor.matmul(h_ps[u % NH][:, :], w1T[:, c, j, :], part[:, c, tokens],
                                              start=(c == 0 and k == 0), stop=(c == NC - 1 and k == 1))
                mm.then_inc(h_done, 1)

            def down(b):
                g, t = divmod(b, BPG)
                pe.wait_ge(lo_done, (g + 1) * FC)
                if b == 0:
                    pe.wait_ge(wT_done, 4)
                    pe.wait_ge(x1_done, B)
                if b >= 2:
                    pe.wait_ge(out_done, b - 1)
                tokens = slice(t * D, (t + 1) * D)
                for j in range(FC):
                    for k, part in enumerate((act_hi, act_lo)):
                        mm = nc.tensor.matmul(o_ps[b % 2][:, 0:N], part[:, g, j, tokens], w2T[:, j, :],
                                              start=(j == 0 and k == 0), stop=(j == FC - 1 and k == 1))
                mm.then_inc(o_done, 1)

            pe.wait_ge(ident_one, 1)
            ctx_transposes(0)
            scores(0)
            ctx_transposes(1)
            scores(1)
            for b in range(B):
                if b + 2 < B:
                    ctx_transposes(b + 2)
                pv(b)
                if b + 2 < B:
                    scores(b + 2)
                if b == 3:
                    z_transposes(0)
                if b == 5:
                    mean(0)
                    z_transposes(1)
                if b == 6:
                    mean(1)
            pe.wait_ge(ident_ready, 1)
            w1_transposes()
            z_transposes(2)
            for u in range(FC):
                up(u)
                if u == 1:
                    z_transposes(3)
            for h in range(2):
                w2_transposes(h)
            for u in range(FC, 2 * FC):
                up(u)
            for b in range(B):
                down(b)


_INS = ["x", "ctx_2048", "g_xattn", "g_ffn", "L0_ffn_w1", "L0_ffn_b1", "L0_ffn_w2", "L0_ffn_b2"]


def kernel(**inputs):
    import numpy as np
    import concourse.bacc as bacc
    from concourse.bass_utils import run_bass_kernel_spmd

    nc = bacc.Bacc("TRN2", target_bir_lowering=False, num_devices=1)
    arrays, args = {}, []
    for name in _INS:
        a = np.ascontiguousarray(inputs[name])
        arrays[f"in_{name}"] = a
        args.append(nc.dram_tensor(f"in_{name}", a.shape, mybir.dt.from_np(a.dtype), kind="ExternalInput").ap())
    shape = inputs["x"].shape
    args.append(nc.dram_tensor("out_x", shape, F32, kind="ExternalOutput").ap())
    flamingo_gated_block(nc, *args)
    r = run_bass_kernel_spmd(nc, [arrays], core_ids=[0])
    return r.results[0]["out_x"]
```

```python
from contextlib import ExitStack

import concourse.bass as bass
from concourse import mybir

F32 = mybir.dt.float32
F32R = mybir.dt.float32r
BF16 = mybir.dt.bfloat16
ALU = mybir.AluOpType
ACT = mybir.ActivationFunctionType

P = 128


def flamingo_gated_block(
    nc: bass.Bass,
    x: bass.AP,
    ctx_kv: bass.AP,
    g_xattn: bass.AP,
    g_ffn: bass.AP,
    w1: bass.AP,
    b1: bass.AP,
    w2: bass.AP,
    b2: bass.AP,
    out: bass.AP,
):
    B, D, N = x.shape
    F = w1.shape[0]
    NC = N // P
    FC = F // P
    TOKENS = B * D
    PAIRS = B // 2
    HALF_W = FC // 2
    UNIT = 512
    Q_ON_POOL = 4
    Z_ON_POOL = 6
    GROUPS = [(0, 2), (2, 4), (4, 8)]
    units = []
    first_unit = []
    for a, b in GROUPS:
        first_unit.append(len(units))
        slots = UNIT // ((b - a) * D)
        units += [(a, b, range(j, j + slots)) for j in range(0, FC, slots)]
    NU = len(units)
    SM_SCALE = float(D) ** -0.5
    LN_EPS = 1e-5
    QUANT_EPS = 1e-8
    WARM_UPS = 8
    HALF_MEAN = 0.5 / (F * N)
    assert D == P and N == 2 * P and F % (2 * P) == 0 and all((b - a) * D <= UNIT for a, b in GROUPS)

    with ExitStack() as stack:
        def sb(name, shape, dt=F32):
            return stack.enter_context(nc.sbuf_tensor(name, shape, dt))

        def sem(name):
            return stack.enter_context(nc.semaphore(name))

        x_sb = sb("x_sb", [P, B, N])
        c_sb = sb("c_sb", [P, B, N])
        w1_sb = sb("w1_sb", [P, FC, N])
        w2_sb = sb("w2_sb", [P, NC, F])
        b1_sb = sb("b1_sb", [P, FC])
        b2_sb = sb("b2_sb", [P, N])
        gates = sb("gates", [P, 2])
        ident = sb("ident", [P, P])
        ident16 = sb("ident16", [P, P], BF16)
        ones = sb("ones", [P, P])
        neg_half = sb("neg_half", [P, B])
        warm = sb("warm", [P, UNIT], BF16)
        stats1 = sb("stats1", [P, B, 6])
        mv1 = sb("mv1", [P, B, 2])
        var1 = sb("var1", [P, B])
        neg_mean1 = sb("neg_mean1", [P, B])
        rstd1 = sb("rstd1", [P, B])
        q_sb = sb("q_sb", [P, B, N])
        ctxT = sb("ctxT", [P, B, NC, P])
        PR = 3
        probs = sb("probs", [P, PR, NC, N])
        tg = sb("tg", [P, 2])
        x1 = sb("x1", [P, B, N])
        stats2 = sb("stats2", [P, B, 6])
        mv2 = sb("mv2", [P, B, 2])
        var2 = sb("var2", [P, B])
        neg_mean2 = sb("neg_mean2", [P, B])
        rstd2 = sb("rstd2", [P, B])
        z_sb = sb("z_sb", [P, B, N])
        zT_hi = sb("zT_hi", [P, NC, TOKENS], F32R)
        zT_lo = sb("zT_lo", [P, NC, TOKENS], F32R)
        w1_abs = sb("w1_abs", [P, F * N // P])
        row_abs = sb("row_abs", [P, 2, 2])
        thr = sb("thr", [P, 2])
        large = sb("large", [P, F * N // P], BF16)
        t1 = sb("t1", [P, FC, N], BF16)
        t2 = sb("t2", [P, NC, F], BF16)
        w_sign = sb("w_sign", [P, 2, F * N // P], BF16)
        w1T = sb("w1T", [P, FC, NC, P], F32R)
        w2T = sb("w2T", [P, FC, N], F32R)
        GR = 3
        act = sb("act", [P, GR, UNIT])
        act_hi = sb("act_hi", [P, NU, UNIT], F32R)
        act_lo = sb("act_lo", [P, NU, UNIT], F32R)
        b2g = sb("b2g", [P, N])
        x1b = x_sb
        out_sb = q_sb

        banks = [stack.enter_context(nc.psum_tensor(f"bank{i}", [P, 512], F32)) for i in range(8)]
        score_ps = [banks[0], banks[1]]
        pv_ps = [banks[2], banks[3]]
        tr_ps = [banks[4], banks[5]]
        z_ps = [banks[6], banks[7], banks[6], banks[7]]
        mean_ps = [banks[7], banks[7]]
        wt_ps = [banks[4], banks[5], banks[5], banks[4]]
        h_ps = [banks[0], banks[1], banks[2], banks[3]]
        NH = len(h_ps)
        o_ps = [banks[6], banks[7]]

        x_loads = [(0, 1), (1, 2), (2, 4), (4, 6), (6, 8)]
        load_of = [next(i for i, (a, b) in enumerate(x_loads) if a <= n < b) for n in range(B)]
        x_in = [sem(f"x_in{i}") for i in range(len(x_loads))]
        c_in = [sem(f"c_in{i}") for i in range(len(x_loads))]
        w1_in, w2_in = sem("w1_in"), sem("w2_in")
        g1_in, g2_in, b1_in, b2_in = sem("g1_in"), sem("g2_in"), sem("b1_in"), sem("b2_in")
        warm_zero, ident_zero, ident_one, ident_ready, const_ready = (
            sem("warm_zero"), sem("ident_zero"), sem("ident_one"), sem("ident_ready"), sem("const_ready"))
        stats1_done, mv1_done, var1_done, rstd1_done, q_done = (
            sem("stats1_done"), sem("mv1_done"), sem("var1_done"), sem("rstd1_done"), sem("q_done"))
        ctx_tr, ctxT_done = sem("ctx_tr"), sem("ctxT_done")
        scores_done, probs_done, pv_done = sem("scores_done"), sem("probs_done"), sem("pv_done")
        tg_done, x1_done = sem("tg_done"), sem("x1_done")
        stats2_done, mv2_done, var2_done, rstd2_done, z_done = (
            sem("stats2_done"), sem("mv2_done"), sem("var2_done"), sem("rstd2_done"), sem("z_done"))
        neg1_done, neg2_done, q_pool, z_pool = sem("neg1_done"), sem("neg2_done"), sem("q_pool"), sem("z_pool")
        z_tr, zhi_done, zlo_done = sem("z_tr"), sem("zhi_done"), sem("zlo_done")
        abs_done, mean_done, thr_done = sem("abs_done"), sem("mean_done"), sem("thr_done")
        sign_done, large_done, tern_done = sem("sign_done"), sem("large_done"), sem("tern_done")
        tern2_done = sem("tern2_done")
        tern2v_done = sem("tern2v_done")
        hi2_done = sem("hi2_done")
        w_tr, wT_done = sem("w_tr"), sem("wT_done")
        h_done, act_done, hi_done, lo_done = sem("h_done"), sem("act_done"), sem("hi_done"), sem("lo_done")
        b2g_done, x1b_done, o_done, out_done, stored = (
            sem("b2g_done"), sem("x1b_done"), sem("o_done"), sem("out_done"), sem("stored"))

        x_dram = x.rearrange("b d n -> d b n")
        c_dram = ctx_kv.rearrange("b d n -> d b n")
        out_dram = out.rearrange("b d n -> d b n")
        w1_dram = w1.rearrange("(p j) n -> p j n", j=FC)
        b1_dram = b1.rearrange("(p j) -> p j", j=FC)
        w2_dram = w2.rearrange("(c p) f -> p c f", p=P)

        WCOLS = F * N // P
        w1_flat = w1_sb[:, :, :].rearrange("p j n -> p (j n)")
        w2_flat = w2_sb[:, :, :].rearrange("p c f -> p (c f)")
        t1_flat = t1[:, :, :].rearrange("p j n -> p (j n)")
        t2_flat = t2[:, :, :].rearrange("p c f -> p (c f)")
        HI_ON_VECTOR = [0, 1, 2, 3, 4, 5, NU - 1]
        hi_count = [sum(v not in HI_ON_VECTOR for v in range(u + 1)) for u in range(NU)]

        w_flat = [w1_flat, w2_flat]
        abs_flat = [w1_abs[:, :], w1_flat]

        block = stack.enter_context(nc.Block())

        @block.sync
        def _(sp):
            def load_batches(i):
                a, b = x_loads[i]
                sp.dma_start(x_sb[:, a:b, :], x_dram[:, a:b, :]).then_inc(x_in[i], 16)
                sp.dma_start(c_sb[:, a:b, :], c_dram[:, a:b, :]).then_inc(c_in[i], 16)

            load_batches(0)
            load_batches(1)
            load_batches(2)
            load_batches(3)
            sp.dma_start(w1_sb[:, :, :], w1_dram).then_inc(w1_in, 16)
            load_batches(4)
            sp.dma_start(w2_sb[:, :, :], w2_dram).then_inc(w2_in, 16)
            sp.dma_start(b1_sb[:, :], b1_dram).then_inc(b1_in, 16)
            sp.dma_start(b2_sb[:, :], b2.partition_broadcast(P)).then_inc(b2_in, 16)
            for b in range(B):
                sp.wait_ge(out_done, b + 1)
                sp.dma_start(out_dram[:, b, :], out_sb[:, b, :]).then_inc(stored, 16)
            sp.wait_ge(stored, 16 * B)

        @block.gpsimd
        def _(pool):
            nc.gpsimd.memset(ident[:, :], 0.0).then_inc(ident_zero, 1)
            nc.gpsimd.memset(neg_half[:, :], -0.5).then_inc(const_ready, 1)
            pool.wait_ge(ident_zero, 1)
            nc.gpsimd.affine_select(out=ident[:, :], in_=ident[:, :], compare_op=ALU.not_equal, fill=1.0,
                                    base=0, pattern=[[-1, P]], channel_multiplier=1).then_inc(ident_one, 1)
            pool.dma_start(gates[:, 0:1], g_xattn.partition_broadcast(P)).then_inc(g1_in, 16)
            pool.dma_start(gates[:, 1:2], g_ffn.partition_broadcast(P)).then_inc(g2_in, 16)

            def rstd(mv, var, r, mv_sem, var_sem, r_sem, a, b):
                pool.wait_ge(mv_sem, b)
                nc.gpsimd.tensor_scalar(var[:, a:b], mv[:, a:b, 1], LN_EPS, None, ALU.add).then_inc(var_sem, b - a)
                pool.wait_ge(var_sem, b)
                pool.wait_ge(const_ready, 1)
                nc.gpsimd.tensor_tensor(r[:, a:b], var[:, a:b], neg_half[:, a:b], ALU.pow).then_inc(r_sem, b - a)

            def normed(dst, src, mv, neg_mean, r, neg_sem, r_sem, d_sem, first, a, b):
                nc.gpsimd.tensor_scalar(neg_mean[:, a:b], mv[:, a:b, 0], -1.0, 1.0, ALU.mult,
                                        ALU.mult).then_inc(neg_sem, b - a)
                pool.wait_ge(r_sem, b)
                pool.wait_ge(neg_sem, b - first)
                for n in range(a, b):
                    nc.gpsimd.tensor_scalar(dst[:, n, :], src[:, n, :], neg_mean[:, n:n + 1], r[:, n:n + 1],
                                            ALU.add, ALU.mult).then_inc(d_sem, 1)

            def queries(a, b):
                rstd(mv1, var1, rstd1, mv1_done, var1_done, rstd1_done, a, b)
                if a >= Q_ON_POOL:
                    normed(q_sb, x_sb, mv1, neg_mean1, rstd1, neg1_done, rstd1_done, q_pool, Q_ON_POOL, a, b)

            def ternary2(h):
                part = slice(h * WCOLS // 2, (h + 1) * WCOLS // 2)
                pool.wait_ge(large_done, 3 + h)
                pool.wait_ge(sign_done, 3 + h)
                nc.gpsimd.tensor_tensor(t2_flat[:, part], large[:, part], w_sign[:, 1, part],
                                        ALU.mult).then_inc(tern2_done, 1)

            for a, b in x_loads[:4]:
                queries(a, b)
            for b in range(Z_ON_POOL):
                rstd(mv2, var2, rstd2, mv2_done, var2_done, rstd2_done, b, b + 1)
                normed(z_sb, x1, mv2, neg_mean2, rstd2, neg2_done, rstd2_done, z_pool, 0, b, b + 1)
                if b == 0:
                    queries(*x_loads[4])
            for b in range(Z_ON_POOL, B):
                rstd(mv2, var2, rstd2, mv2_done, var2_done, rstd2_done, b, b + 1)
            ternary2(0)
            pool.wait_ge(b2_in, 16)
            pool.wait_ge(tg_done, 1)
            nc.gpsimd.tensor_scalar(b2g[:, :], b2_sb[:, :], tg[:, 1:2], 1.0, ALU.mult, ALU.mult).then_inc(b2g_done, 1)
            pool.wait_ge(b2g_done, 1)
            for b in range(B):
                pool.wait_ge(x1_done, b + 1)
                nc.gpsimd.tensor_tensor(x1b[:, b, :], x1[:, b, :], b2g[:, :], ALU.add).then_inc(x1b_done, 1)

        @block.scalar
        def _(act_e):
            nc.scalar.preload_act_table(ACT.Sigmoid)

            def ctxT_copy(b):
                act_e.wait_ge(ctx_tr, b + 1)
                nc.scalar.activation(ctxT[:, b, :, :], tr_ps[b % 2][:, 0:N].rearrange("p (c v) -> p c v", c=NC),
                                     ACT.Copy).then_inc(ctxT_done, 1)

            def sigmoid(b):
                act_e.wait_ge(scores_done, b + 1)
                if b >= PR:
                    act_e.wait_ge(pv_done, b - PR + 1)
                nc.scalar.activation(probs[:, b % PR, :, :], score_ps[b % 2][:, :].rearrange("p (c m) -> p c m", c=NC),
                                     ACT.Sigmoid, scale=SM_SCALE).then_inc(probs_done, 1)

            def z_hi(k):
                act_e.wait_ge(z_tr, k + 1)
                nc.scalar.activation(
                    zT_hi[:, :, 2 * k * P:(2 * k + 2) * P].rearrange("p c (b t) -> p b c t", b=2),
                    z_ps[k][:, :].rearrange("p (b c t) -> p b c t", b=2, c=NC), ACT.Copy).then_inc(zhi_done, 1)

            def abs_sum(i, h):
                act_e.wait_ge((w1_in, w2_in)[i], 16)
                part = slice(h * WCOLS // 2, (h + 1) * WCOLS // 2)
                if i == 1:
                    act_e.wait_ge(sign_done, 2)
                nc.scalar.activation(abs_flat[i][:, part], w_flat[i][:, part], ACT.Abs,
                                     accum_out=row_abs[:, i, h:h + 1]).then_inc(abs_done, 1)

            def sign(i, h):
                part = slice(h * WCOLS // 2, (h + 1) * WCOLS // 2)
                nc.scalar.activation(w_sign[:, i, part], w_flat[i][:, part],
                                     ACT.Sign).then_inc(sign_done, 1)

            def wT_copy(dst, i):
                act_e.wait_ge(w_tr, i + 1)
                nc.scalar.activation(dst, wt_ps[i][:, :].bitcast(BF16), ACT.Copy).then_inc(wT_done, 1)

            def gelu(u):
                a, b, slots = units[u]
                n = (b - a) * D
                act_e.wait_ge(h_done, u + 1)
                if u == 0:
                    act_e.wait_ge(b1_in, 16)
                if u >= GR:
                    act_e.wait_ge(lo_done, u - GR + 1)
                for i, j in enumerate(slots):
                    op = nc.scalar.activation(act[:, u % GR, i * n:(i + 1) * n], h_ps[u % NH][:, i * n:(i + 1) * n],
                                              ACT.Gelu, bias=b1_sb[:, j:j + 1])
                op.then_inc(act_done, 1)
                if u not in HI_ON_VECTOR:
                    for i, j in enumerate(slots):
                        op = nc.scalar.activation(act_hi[:, u, i * n:(i + 1) * n], h_ps[u % NH][:, i * n:(i + 1) * n],
                                                  ACT.Gelu, bias=b1_sb[:, j:j + 1])
                    op.then_inc(hi_done, 1)

            for s in range(B):
                ctxT_copy(s)
                sigmoid(s)
                if s == 0:
                    act_e.wait_ge(g1_in, 16)
                    act_e.wait_ge(g2_in, 16)
                    nc.scalar.activation(tg[:, :], gates[:, :], ACT.Tanh).then_inc(tg_done, 1)
                if s in (2, 3):
                    abs_sum(0, s - 2)
                if s in (3, 4):
                    sign(0, s - 3)
                if s == 6:
                    z_hi(0)
                if s in (5, 6):
                    abs_sum(1, s - 5)
            wT_copy(w1T[:, 0:HALF_W, :, :].rearrange("p j c f -> p (j c f)"), 0)
            nc.scalar.preload_act_table(ACT.Gelu)
            wT_copy(w1T[:, HALF_W:FC, :, :].rearrange("p j c f -> p (j c f)"), 1)
            z_hi(1)
            sign(1, 0)
            gelu(0)
            sign(1, 1)
            for u in range(1, NU):
                gelu(u)
                if u == 2:
                    z_hi(2)
                    z_hi(3)
                if u == 3:
                  for h in (0, 1):
                    wT_copy(w2T[:, h * HALF_W:(h + 1) * HALF_W, :].rearrange("p j d -> p (j d)"), 2 + h)

        @block.vector
        def _(dve):
            nc.vector.memset(warm[:, :], 0.0).then_inc(warm_zero, 1)
            nc.vector.memset(ones[:, :], 1.0).then_inc(const_ready, 1)
            dve.wait_ge(ident_one, 1)
            nc.vector.tensor_copy(ident16[:, :], ident[:, :]).then_inc(ident_ready, 1)

            def ln_stats(src, stats, mv, s_sem, mv_sem, b, between=None):
                nc.vector.bn_stats(stats[:, b, :], src[:, b, :]).then_inc(s_sem, 1)
                if between:
                    between()
                dve.wait_ge(s_sem, b + 1)
                nc.vector.bn_aggr(mv[:, b, :], stats[:, b, :]).then_inc(mv_sem, 1)

            def stats_x(b):
                dve.wait_ge(x_in[load_of[b]], 16)
                ln_stats(x_sb, stats1, mv1, stats1_done, mv1_done, b)

            def normed(dst, src, mv, r, r_sem, d_sem, b):
                dve.wait_ge(r_sem, b + 1)
                nc.vector.tensor_scalar(dst[:, b, :], src[:, b, :], mv[:, b, 0:1], r[:, b:b + 1],
                                        ALU.subtract, ALU.mult).then_inc(d_sem, 1)

            def q_of(b):
                normed(q_sb, x_sb, mv1, rstd1, rstd1_done, q_done, b)

            def residual1(b, before, between):
                before()
                dve.wait_ge(pv_done, b + 1)
                dve.wait_ge(tg_done, 1)
                nc.vector.scalar_tensor_tensor(out=x1[:, b, :], in0=pv_ps[b % 2][:, 0:N], scalar=tg[:, 0:1],
                                               in1=x_sb[:, b, :], op0=ALU.mult, op1=ALU.add).then_inc(x1_done, 1)
                dve.wait_ge(x1_done, b + 1)
                ln_stats(x1, stats2, mv2, stats2_done, mv2_done, b, between)

            def z_of(b):
                normed(z_sb, x1, mv2, rstd2, rstd2_done, z_done, b)

            def z_lo(k):
                dve.wait_ge(zhi_done, k + 1)
                tokens = slice(2 * k * P, (2 * k + 2) * P)
                nc.vector.tensor_tensor(
                    zT_lo[:, :, tokens].rearrange("p c (b t) -> p b c t", b=2),
                    z_ps[k][:, :].rearrange("p (b c t) -> p b c t", b=2, c=NC),
                    zT_hi[:, :, tokens].bitcast(F32).rearrange("p c (b t) -> p b c t", b=2),
                    ALU.subtract).then_inc(zlo_done, 1)

            def threshold(i):
                dve.wait_ge(mean_done, i + 1)
                nc.vector.tensor_scalar(thr[:, i:i + 1], mean_ps[i][:, 0:1], HALF_MEAN, 0.5 * QUANT_EPS,
                                        ALU.mult, ALU.max).then_inc(thr_done, 1)

            def mask(i, h):
                part = slice(h * WCOLS // 2, (h + 1) * WCOLS // 2)
                dve.wait_ge(thr_done, i + 1)
                if i == 1:
                    dve.wait_ge(tern_done, h + 1)
                nc.vector.tensor_scalar(large[:, part], abs_flat[i][:, part], thr[:, i:i + 1], None,
                                        ALU.is_gt).then_inc(large_done, 1)

            def ternary1(h):
                part = slice(h * WCOLS // 2, (h + 1) * WCOLS // 2)
                dve.wait_ge(large_done, h + 1)
                dve.wait_ge(sign_done, h + 1)
                nc.vector.tensor_tensor(t1_flat[:, part], large[:, part], w_sign[:, 0, part],
                                        ALU.mult).then_inc(tern_done, 1)

            def ternary2(h):
                part = slice(h * WCOLS // 2, (h + 1) * WCOLS // 2)
                dve.wait_ge(large_done, 3 + h)
                dve.wait_ge(sign_done, 3 + h)
                nc.vector.tensor_tensor(t2_flat[:, part], large[:, part], w_sign[:, 1, part],
                                        ALU.mult).then_inc(tern2v_done, 1)

            def act_copy(u):
                dve.wait_ge(act_done, u + 1)
                nc.vector.tensor_copy(act_hi[:, u, :], act[:, u % GR, :]).then_inc(hi2_done, 1)

            def act_rest(u):
                if u in HI_ON_VECTOR:
                    dve.wait_ge(hi2_done, HI_ON_VECTOR.index(u) + 1)
                else:
                    dve.wait_ge(hi_done, hi_count[u])
                nc.vector.tensor_tensor(act_lo[:, u, :], act[:, u % GR, :], act_hi[:, u, :].bitcast(F32),
                                        ALU.subtract).then_inc(lo_done, 1)

            def residual2(b):
                dve.wait_ge(o_done, b + 1)
                dve.wait_ge(x1b_done, b + 1)
                nc.vector.scalar_tensor_tensor(out=out_sb[:, b, :], in0=o_ps[b % 2][:, 0:N], scalar=tg[:, 1:2],
                                               in1=x1b[:, b, :], op0=ALU.mult, op1=ALU.add).then_inc(out_done, 1)

            stats_x(0)
            stats_x(1)
            q_of(0)
            stats_x(2)
            q_of(1)
            stats_x(3)
            q_of(2)
            q_of(3)
            stats_x(4)
            stats_x(5)

            def before(b):
                if b == 1:
                    stats_x(6)
                    stats_x(7)
                if b == 2:
                    threshold(0)
                    mask(0, 0)
                if b == 3:
                    mask(0, 1)
                    ternary1(0)
                if b == 4:
                    ternary1(1)
                if b == 6:
                    threshold(1)

            def between(b):
                if b == 5:
                    z_lo(0)
                if b == 6:
                    mask(1, 0)

            for b in range(B):
                residual1(b, lambda: before(b), lambda: between(b))
            z_lo(1)
            mask(1, 1)
            for b in range(Z_ON_POOL, B):
                z_of(b)
            for u in range(NU):
                if u % 2 == 0 and u in HI_ON_VECTOR:
                    act_copy(u)
                    if u == 0:
                        ternary2(1)
                    act_copy(u + 1)
                if u == NU - 1:
                    act_copy(u)
                act_rest(u)
                if u == 3:
                    z_lo(2)
                    z_lo(3)
                if u == 6:
                    residual2(0)
                if u == 11:
                    residual2(1)
                if u == 14:
                    residual2(2)
            for b in range(3, B):
                residual2(b)

        @block.tensor
        def _(pe):
            def ctx_transposes(b):
                pe.wait_ge(c_in[load_of[b]], 16)
                if b >= 2:
                    pe.wait_ge(ctxT_done, b - 1)
                for c in range(NC):
                    mm = nc.tensor.transpose(tr_ps[b % 2][:, c * P:(c + 1) * P], c_sb[:, b, c * P:(c + 1) * P],
                                             ident[:, :])
                mm.then_inc(ctx_tr, 1)

            def scores(b):
                if b < Q_ON_POOL:
                    pe.wait_ge(q_done, b + 1)
                else:
                    pe.wait_ge(q_pool, b + 1 - Q_ON_POOL)
                if b >= 2:
                    pe.wait_ge(probs_done, b - 1)
                for c in range(NC):
                    mm = nc.tensor.matmul(score_ps[b % 2][:, c * N:(c + 1) * N], q_sb[:, b, c * P:(c + 1) * P],
                                          c_sb[:, b, :], start=True, stop=True)
                mm.then_inc(scores_done, 1)

            def pv(b):
                pe.wait_ge(ctxT_done, b + 1)
                pe.wait_ge(probs_done, b + 1)
                if b >= 2:
                    pe.wait_ge(x1_done, b - 1)
                for c in range(NC):
                    mm = nc.tensor.matmul(pv_ps[b % 2][:, 0:N], ctxT[:, b, c, :], probs[:, b % PR, c, :],
                                          start=(c == 0), stop=(c == NC - 1))
                mm.then_inc(pv_done, 1)

            def z_transposes(k):
                if 2 * k < Z_ON_POOL:
                    pe.wait_ge(z_pool, 2 * k + 2)
                else:
                    pe.wait_ge(z_done, 2 * k + 2 - Z_ON_POOL)
                if k == 1:
                    pe.wait_ge(thr_done, 2)
                if k >= 2:
                    pe.wait_ge(zlo_done, k - 1)
                for b in range(2):
                    for c in range(NC):
                        mm = nc.tensor.transpose(z_ps[k][:, (2 * b + c) * P:(2 * b + c + 1) * P],
                                                 z_sb[:, 2 * k + b, c * P:(c + 1) * P], ident[:, :])
                mm.then_inc(z_tr, 1)

            def mean(i):
                pe.wait_ge(abs_done, 2 * i + 2)
                pe.wait_ge(const_ready, 2)
                if i == 1:
                    pe.wait_ge(thr_done, 1)
                for h in range(2):
                    mm = nc.tensor.matmul(mean_ps[i][:, 0:1], ones[:, :], row_abs[:, i, h:h + 1], start=(h == 0),
                                          stop=(h == 1))
                mm.then_inc(mean_done, 1)

            def w1_transposes(h):
                pe.wait_ge(tern_done, h + 1)
                pe.wait_ge(ctxT_done, B - 1 + h)
                for j in range(HALF_W):
                    for c in range(NC):
                        mm = nc.tensor.transpose(wt_ps[h][:, :].bitcast(BF16)[:, (j * NC + c) * P:(j * NC + c + 1) * P],
                                                 t1[:, h * HALF_W + j, c * P:(c + 1) * P], ident16[:, :])
                mm.then_inc(w_tr, 1)

            def w2_transposes(h):
                pe.wait_ge(tern2_done, 1)
                pe.wait_ge(tern2v_done, 1)
                pe.wait_ge(wT_done, 2 - h)
                by_slot = t2[:, :, :].rearrange("p c (f j) -> p c j f", j=FC)
                for j in range(HALF_W):
                    for c in range(NC):
                        mm = nc.tensor.transpose(
                            wt_ps[2 + h][:, :].bitcast(BF16)[:, (j * NC + c) * P:(j * NC + c + 1) * P],
                            by_slot[:, c, h * HALF_W + j, :], ident16[:, :])
                mm.then_inc(w_tr, 1)

            def up(u):
                a, b, slots = units[u]
                n = (b - a) * D
                pe.wait_ge(zlo_done, b // 2)
                pe.wait_ge(wT_done, 1 + slots[-1] // HALF_W)
                if u >= NH:
                    pe.wait_ge(act_done, u - NH + 1)
                    if u - NH not in HI_ON_VECTOR:
                        pe.wait_ge(hi_done, hi_count[u - NH])
                elif u < 2:
                    pe.wait_ge(probs_done, B)
                else:
                    pe.wait_ge(x1_done, B + u - 3)
                for i, j in enumerate(slots):
                    for c in range(NC):
                        for k, part in enumerate((zT_hi, zT_lo)):
                            mm = nc.tensor.matmul(h_ps[u % NH][:, i * n:(i + 1) * n], w1T[:, j, c, :],
                                                  part[:, c, a * D:b * D],
                                                  start=(c == 0 and k == 0), stop=(c == NC - 1 and k == 1))
                mm.then_inc(h_done, 1)

            def down(b):
                g = next(i for i, (a, e) in enumerate(GROUPS) if a <= b < e)
                a, e = GROUPS[g]
                n = (e - a) * D
                last = first_unit[g + 1] if g + 1 < len(GROUPS) else NU
                pe.wait_ge(lo_done, last)
                if b == 0:
                    pe.wait_ge(wT_done, 4)
                if b < 2:
                    pe.wait_ge(zlo_done, 3 + b)
                if b >= 2:
                    pe.wait_ge(out_done, b - 1)
                for j in range(FC):
                    u, i = divmod(j * n, UNIT)
                    at = i + (b - a) * D
                    for k, part in enumerate((act_hi, act_lo)):
                        mm = nc.tensor.matmul(o_ps[b % 2][:, 0:N], part[:, first_unit[g] + u, at:at + D], w2T[:, j, :],
                                              start=(j == 0 and k == 0), stop=(j == FC - 1 and k == 1))
                mm.then_inc(o_done, 1)

            pe.wait_ge(warm_zero, 1)
            for _ in range(WARM_UPS):
                nc.tensor.matmul(o_ps[1][:, :], warm[:, 0:P], warm[:, :], start=True, stop=True)
            pe.wait_ge(ident_one, 1)
            for s in range(B):
                ctx_transposes(s)
                scores(s)
                if s >= 2:
                    pv(s - 2)
                if s == 4:
                    mean(0)
                if s == 6:
                    z_transposes(0)
            mean(1)
            pe.wait_ge(ident_ready, 1)
            w1_transposes(0)
            pv(B - 2)
            w1_transposes(1)
            z_transposes(1)
            pv(B - 1)
            for u in range(4):
                up(u)
            z_transposes(2)
            z_transposes(3)
            up(4)
            w2_transposes(0)
            w2_transposes(1)
            up(5)
            up(6)
            u = 7
            for b, ups in enumerate((4, 3, 2)):
                down(b)
                for u in range(u, u + ups):
                    up(u)
                u += 1
            for b in range(3, B):
                down(b)


_INS = ["x", "ctx_2048", "g_xattn", "g_ffn", "L0_ffn_w1", "L0_ffn_b1", "L0_ffn_w2", "L0_ffn_b2"]


def kernel(**inputs):
    import numpy as np
    import concourse.bacc as bacc
    from concourse.bass_utils import run_bass_kernel_spmd

    nc = bacc.Bacc("TRN2", target_bir_lowering=False, num_devices=1)
    arrays, args = {}, []
    for name in _INS:
        a = np.ascontiguousarray(inputs[name])
        arrays[f"in_{name}"] = a
        args.append(nc.dram_tensor(f"in_{name}", a.shape, mybir.dt.from_np(a.dtype), kind="ExternalInput").ap())
    shape = inputs["x"].shape
    args.append(nc.dram_tensor("out_x", shape, F32, kind="ExternalOutput").ap())
    flamingo_gated_block(nc, *args)
    r = run_bass_kernel_spmd(nc, [arrays], core_ids=[0])
    return r.results[0]["out_x"]
```

```python
from contextlib import ExitStack

import concourse.bass as bass
from concourse import mybir

F32 = mybir.dt.float32
F32R = mybir.dt.float32r
BF16 = mybir.dt.bfloat16
ALU = mybir.AluOpType
ACT = mybir.ActivationFunctionType

P = 128


def flamingo_gated_block(
    nc: bass.Bass,
    x: bass.AP,
    ctx_kv: bass.AP,
    g_xattn: bass.AP,
    g_ffn: bass.AP,
    w1: bass.AP,
    b1: bass.AP,
    w2: bass.AP,
    b2: bass.AP,
    out: bass.AP,
):
    B, D, N = x.shape
    F = w1.shape[0]
    NC = N // P
    FC = F // P
    TOKENS = B * D
    HALF_W = FC // 2
    UNIT = 512
    Q_ON_POOL = 4
    Z_ON_POOL = 6
    GROUPS = [(0, 2), (2, 4), (4, 8)]
    units = []
    first_unit = []
    for a, b in GROUPS:
        first_unit.append(len(units))
        slots = UNIT // ((b - a) * D)
        units += [(a, b, range(j, j + slots)) for j in range(0, FC, slots)]
    NU = len(units)
    SM_SCALE = float(D) ** -0.5
    LN_EPS = 1e-5
    QUANT_EPS = 1e-8
    WARM_UPS = 7
    HALF_MEAN = 0.5 / (F * N)
    assert D == P and N == 2 * P and F % (2 * P) == 0 and all((b - a) * D <= UNIT for a, b in GROUPS)

    with ExitStack() as stack:
        def sb(name, shape, dt=F32):
            return stack.enter_context(nc.sbuf_tensor(name, shape, dt))

        def sem(name):
            return stack.enter_context(nc.semaphore(name))

        x_sb = sb("x_sb", [P, B, N])
        c_sb = sb("c_sb", [P, B, N])
        w1_sb = sb("w1_sb", [P, FC, N])
        w2_sb = sb("w2_sb", [P, NC, F])
        b1_sb = sb("b1_sb", [P, FC])
        b2_sb = sb("b2_sb", [P, N])
        gates = sb("gates", [P, 2])
        ident = sb("ident", [P, P])
        ident16 = sb("ident16", [P, P], BF16)
        ones = sb("ones", [P, P])
        neg_half = sb("neg_half", [P, B])
        warm = sb("warm", [P, UNIT], BF16)
        stats1 = sb("stats1", [P, B, 6])
        mv1 = sb("mv1", [P, B, 2])
        var1 = sb("var1", [P, B])
        neg_mean1 = sb("neg_mean1", [P, B])
        rstd1 = sb("rstd1", [P, B])
        q_sb = sb("q_sb", [P, B, N])
        ctxT = sb("ctxT", [P, B, NC, P])
        PR = 3
        probs = sb("probs", [P, PR, NC, N])
        tg = sb("tg", [P, 2])
        x1 = sb("x1", [P, B, N])
        stats2 = sb("stats2", [P, B, 6])
        mv2 = sb("mv2", [P, B, 2])
        var2 = sb("var2", [P, B])
        neg_mean2 = sb("neg_mean2", [P, B])
        rstd2 = sb("rstd2", [P, B])
        z_sb = sb("z_sb", [P, B, N])
        zT_hi = sb("zT_hi", [P, NC, TOKENS], F32R)
        zT_lo = sb("zT_lo", [P, NC, TOKENS], F32R)
        w1_abs = sb("w1_abs", [P, F * N // P])
        row_abs = sb("row_abs", [P, 2, 2])
        sum_abs = sb("sum_abs", [P, 2])
        thr = sb("thr", [P, 2])
        large = sb("large", [P, F * N // P], BF16)
        t1 = sb("t1", [P, FC, N], BF16)
        t2 = sb("t2", [P, NC, F], BF16)
        w_sign = sb("w_sign", [P, 2, F * N // P], BF16)
        w1T = sb("w1T", [P, FC, NC, P], F32R)
        w2T = sb("w2T", [P, FC, N], F32R)
        GR = 3
        act = sb("act", [P, GR, UNIT])
        act_hi = sb("act_hi", [P, NU, UNIT], F32R)
        act_lo = sb("act_lo", [P, NU, UNIT], F32R)
        b2g = sb("b2g", [P, N])
        x1b = x_sb
        out_sb = q_sb

        banks = [stack.enter_context(nc.psum_tensor(f"bank{i}", [P, 512], F32)) for i in range(8)]
        score_ps = [banks[0], banks[1]]
        pv_ps = [banks[2], banks[3]]
        tr_ps = [banks[4], banks[5]]
        z_ps = [banks[6], banks[7], banks[6], banks[7]]
        mean_ps = banks[7]
        wt_ps = [banks[4], banks[5], banks[5], banks[4]]
        h_ps = [banks[0], banks[1], banks[2], banks[3]]
        NH = len(h_ps)
        o_ps = [banks[6], banks[7]]

        x_loads = [(0, 1), (1, 2), (2, 4), (4, 6), (6, 8)]
        load_of = [next(i for i, (a, b) in enumerate(x_loads) if a <= n < b) for n in range(B)]
        x_in = [sem(f"x_in{i}") for i in range(len(x_loads))]
        c_in = [sem(f"c_in{i}") for i in range(len(x_loads))]
        w1_in, w2_in = sem("w1_in"), sem("w2_in")
        g1_in, g2_in, b1_in, b2_in = sem("g1_in"), sem("g2_in"), sem("b1_in"), sem("b2_in")
        warm_zero, ident_zero, ident_one, ident_ready, ones_ready, neg_half_ready = (
            sem("warm_zero"), sem("ident_zero"), sem("ident_one"), sem("ident_ready"), sem("ones_ready"),
            sem("neg_half_ready"))
        stats1_done, mv1_done, var1_done, rstd1_done, q_vector = (
            sem("stats1_done"), sem("mv1_done"), sem("var1_done"), sem("rstd1_done"), sem("q_vector"))
        ctx_tr, ctxT_done = sem("ctx_tr"), sem("ctxT_done")
        scores_done, probs_done, pv_done = sem("scores_done"), sem("probs_done"), sem("pv_done")
        tg_done, x1_done = sem("tg_done"), sem("x1_done")
        stats2_done, mv2_done, var2_done, rstd2_done, z_vector = (
            sem("stats2_done"), sem("mv2_done"), sem("var2_done"), sem("rstd2_done"), sem("z_vector"))
        neg1_done, neg2_done, q_pool, z_pool = sem("neg1_done"), sem("neg2_done"), sem("q_pool"), sem("z_pool")
        z_tr, zhi_done, zlo_done = sem("z_tr"), sem("zhi_done"), sem("zlo_done")
        sum_done = sem("sum_done")
        abs_done, mean_done, thr_done = sem("abs_done"), sem("mean_done"), sem("thr_done")
        sign_done, large_done, tern1_done = sem("sign_done"), sem("large_done"), sem("tern1_done")
        tern2_pool = sem("tern2_pool")
        tern2_vector = sem("tern2_vector")
        hi_vector = sem("hi_vector")
        w_tr, wT_done = sem("w_tr"), sem("wT_done")
        h_done, act_done, hi_scalar, lo_done = sem("h_done"), sem("act_done"), sem("hi_scalar"), sem("lo_done")
        b2g_done, x1b_done, o_done, out_done, stored = (
            sem("b2g_done"), sem("x1b_done"), sem("o_done"), sem("out_done"), sem("stored"))

        x_dram = x.rearrange("b d n -> d b n")
        c_dram = ctx_kv.rearrange("b d n -> d b n")
        out_dram = out.rearrange("b d n -> d b n")
        w1_dram = w1.rearrange("(p j) n -> p j n", j=FC)
        b1_dram = b1.rearrange("(p j) -> p j", j=FC)
        w2_dram = w2.rearrange("(c p) f -> p c f", p=P)

        WCOLS = F * N // P
        w1_flat = w1_sb[:, :, :].rearrange("p j n -> p (j n)")
        w2_flat = w2_sb[:, :, :].rearrange("p c f -> p (c f)")
        t1_flat = t1[:, :, :].rearrange("p j n -> p (j n)")
        t2_flat = t2[:, :, :].rearrange("p c f -> p (c f)")
        FIRST_OF_LAST = first_unit[-1]
        HI_ON_VECTOR = [u for u in range(NU) if u < FIRST_OF_LAST or u % 2 == 1]
        hi_count = [sum(v not in HI_ON_VECTOR for v in range(u + 1)) for u in range(NU)]

        w_flat = [w1_flat, w2_flat]
        abs_flat = [w1_abs[:, :], w1_flat]

        block = stack.enter_context(nc.Block())

        @block.sync
        def _(sp):
            def load_batches(i):
                a, b = x_loads[i]
                sp.dma_start(x_sb[:, a:b, :], x_dram[:, a:b, :]).then_inc(x_in[i], 16)
                sp.dma_start(c_sb[:, a:b, :], c_dram[:, a:b, :]).then_inc(c_in[i], 16)

            load_batches(0)
            load_batches(1)
            load_batches(2)
            load_batches(3)
            sp.dma_start(w1_sb[:, :, :], w1_dram).then_inc(w1_in, 16)
            load_batches(4)
            sp.dma_start(w2_sb[:, :, :], w2_dram).then_inc(w2_in, 16)
            sp.dma_start(b1_sb[:, :], b1_dram).then_inc(b1_in, 16)
            sp.dma_start(b2_sb[:, :], b2.partition_broadcast(P)).then_inc(b2_in, 16)
            with sp.Fori(0, B) as b:
                sp.wait_ge(out_done, b + 1)
                sp.dma_start(out_dram[:, b, :], out_sb[:, b, :]).then_inc(stored, 16)
            sp.wait_ge(stored, 16 * B)

        @block.gpsimd
        def _(pool):
            nc.gpsimd.memset(ident[:, :], 0.0).then_inc(ident_zero, 1)
            nc.gpsimd.memset(neg_half[:, :], -0.5).then_inc(neg_half_ready, 1)
            pool.wait_ge(ident_zero, 1)
            nc.gpsimd.affine_select(out=ident[:, :], in_=ident[:, :], compare_op=ALU.not_equal, fill=1.0,
                                    base=0, pattern=[[-1, P]], channel_multiplier=1).then_inc(ident_one, 1)
            pool.dma_start(gates[:, 0:1], g_xattn.partition_broadcast(P)).then_inc(g1_in, 16)
            pool.dma_start(gates[:, 1:2], g_ffn.partition_broadcast(P)).then_inc(g2_in, 16)

            def rstd(mv, var, r, mv_sem, var_sem, r_sem, a, b):
                pool.wait_ge(mv_sem, b)
                nc.gpsimd.tensor_scalar(var[:, a:b], mv[:, a:b, 1], LN_EPS, None, ALU.add).then_inc(var_sem, b - a)
                pool.wait_ge(var_sem, b)
                pool.wait_ge(neg_half_ready, 1)
                nc.gpsimd.tensor_tensor(r[:, a:b], var[:, a:b], neg_half[:, a:b], ALU.pow).then_inc(r_sem, b - a)

            def normed(dst, src, mv, neg_mean, r, neg_sem, r_sem, d_sem, first, a, b):
                nc.gpsimd.tensor_scalar(neg_mean[:, a:b], mv[:, a:b, 0], -1.0, 1.0, ALU.mult,
                                        ALU.mult).then_inc(neg_sem, b - a)
                pool.wait_ge(r_sem, b)
                pool.wait_ge(neg_sem, b - first)
                for n in range(a, b):
                    nc.gpsimd.tensor_scalar(dst[:, n, :], src[:, n, :], neg_mean[:, n:n + 1], r[:, n:n + 1],
                                            ALU.add, ALU.mult).then_inc(d_sem, 1)

            def queries(a, b):
                rstd(mv1, var1, rstd1, mv1_done, var1_done, rstd1_done, a, b)
                if a >= Q_ON_POOL:
                    normed(q_sb, x_sb, mv1, neg_mean1, rstd1, neg1_done, rstd1_done, q_pool, Q_ON_POOL, a, b)

            def ternary2(h):
                part = slice(h * WCOLS // 2, (h + 1) * WCOLS // 2)
                pool.wait_ge(large_done, 3 + h)
                pool.wait_ge(sign_done, 3 + h)
                nc.gpsimd.tensor_tensor(t2_flat[:, part], large[:, part], w_sign[:, 1, part],
                                        ALU.mult).then_inc(tern2_pool, 1)

            for a, b in ((0, 1), (1, 2), (2, 3), (3, 4), (4, 6)):
                queries(a, b)
            for b in range(Z_ON_POOL):
                rstd(mv2, var2, rstd2, mv2_done, var2_done, rstd2_done, b, b + 1)
                normed(z_sb, x1, mv2, neg_mean2, rstd2, neg2_done, rstd2_done, z_pool, 0, b, b + 1)
                if b == 0:
                    queries(6, 8)
            for b in range(Z_ON_POOL, B):
                rstd(mv2, var2, rstd2, mv2_done, var2_done, rstd2_done, b, b + 1)
            ternary2(0)
            pool.wait_ge(b2_in, 16)
            pool.wait_ge(tg_done, 1)
            nc.gpsimd.tensor_scalar(b2g[:, :], b2_sb[:, :], tg[:, 1:2], 1.0, ALU.mult, ALU.mult).then_inc(b2g_done, 1)
            pool.wait_ge(b2g_done, 1)
            with pool.Fori(0, B) as b:
                pool.wait_ge(x1_done, b + 1)
                nc.gpsimd.tensor_tensor(x1b[:, b, :], x1[:, b, :], b2g[:, :], ALU.add).then_inc(x1b_done, 1)

        @block.scalar
        def _(act_e):
            nc.scalar.preload_act_table(ACT.Sigmoid)

            def ctxT_copy(b):
                act_e.wait_ge(ctx_tr, b + 1)
                nc.scalar.activation(ctxT[:, b, :, :], tr_ps[b % 2][:, 0:N].rearrange("p (c v) -> p c v", c=NC),
                                     ACT.Copy).then_inc(ctxT_done, 1)

            def sigmoid(b):
                act_e.wait_ge(scores_done, b + 1)
                if b >= PR:
                    act_e.wait_ge(pv_done, b - PR + 1)
                nc.scalar.activation(probs[:, b % PR, :, :], score_ps[b % 2][:, :].rearrange("p (c m) -> p c m", c=NC),
                                     ACT.Sigmoid, scale=SM_SCALE).then_inc(probs_done, 1)

            def z_hi(k):
                act_e.wait_ge(z_tr, k + 1)
                nc.scalar.activation(
                    zT_hi[:, :, 2 * k * P:(2 * k + 2) * P].rearrange("p c (b t) -> p b c t", b=2),
                    z_ps[k][:, :].rearrange("p (b c t) -> p b c t", b=2, c=NC), ACT.Copy).then_inc(zhi_done, 1)

            def abs_sum(i, h):
                act_e.wait_ge((w1_in, w2_in)[i], 16)
                part = slice(h * WCOLS // 2, (h + 1) * WCOLS // 2)
                if i == 1:
                    act_e.wait_ge(sign_done, 2)
                nc.scalar.activation(abs_flat[i][:, part], w_flat[i][:, part], ACT.Abs,
                                     accum_out=row_abs[:, i, h:h + 1]).then_inc(abs_done, 1)

            def sign(i, h):
                part = slice(h * WCOLS // 2, (h + 1) * WCOLS // 2)
                nc.scalar.activation(w_sign[:, i, part], w_flat[i][:, part],
                                     ACT.Sign).then_inc(sign_done, 1)

            def wT_copy(dst, i):
                act_e.wait_ge(w_tr, i + 1)
                nc.scalar.activation(dst, wt_ps[i][:, :].bitcast(BF16), ACT.Copy).then_inc(wT_done, 1)

            def gelu(u):
                a, b, slots = units[u]
                n = (b - a) * D
                act_e.wait_ge(h_done, u + 1)
                if u == 0:
                    act_e.wait_ge(b1_in, 16)
                if u >= GR:
                    act_e.wait_ge(lo_done, u - GR + 1)
                for i, j in enumerate(slots):
                    op = nc.scalar.activation(act[:, u % GR, i * n:(i + 1) * n], h_ps[u % NH][:, i * n:(i + 1) * n],
                                              ACT.Gelu, bias=b1_sb[:, j:j + 1])
                op.then_inc(act_done, 1)
                if u not in HI_ON_VECTOR:
                    for i, j in enumerate(slots):
                        op = nc.scalar.activation(act_hi[:, u, i * n:(i + 1) * n], h_ps[u % NH][:, i * n:(i + 1) * n],
                                                  ACT.Gelu, bias=b1_sb[:, j:j + 1])
                    op.then_inc(hi_scalar, 1)

            ctxT_copy(0)
            for s in range(B):
                if s + 1 < B:
                    ctxT_copy(s + 1)
                sigmoid(s)
                if s == 0:
                    act_e.wait_ge(g1_in, 16)
                    act_e.wait_ge(g2_in, 16)
                    nc.scalar.activation(tg[:, :], gates[:, :], ACT.Tanh).then_inc(tg_done, 1)
                if s in (2, 3):
                    abs_sum(0, s - 2)
                if s in (3, 4):
                    sign(0, s - 3)
                if s == 6:
                    z_hi(0)
                if s in (5, 6):
                    abs_sum(1, s - 5)
            wT_copy(w1T[:, 0:HALF_W, :, :].rearrange("p j c f -> p (j c f)"), 0)
            nc.scalar.preload_act_table(ACT.Gelu)
            wT_copy(w1T[:, HALF_W:FC, :, :].rearrange("p j c f -> p (j c f)"), 1)
            z_hi(1)
            sign(1, 0)
            gelu(0)
            sign(1, 1)
            for u in range(1, NU):
                gelu(u)
                if u == 2:
                    z_hi(2)
                    z_hi(3)
                if u == 3:
                  for h in (0, 1):
                    wT_copy(w2T[:, h * HALF_W:(h + 1) * HALF_W, :].rearrange("p j d -> p (j d)"), 2 + h)

        @block.vector
        def _(dve):
            nc.vector.memset(warm[:, :], 0.0).then_inc(warm_zero, 1)
            nc.vector.memset(ones[:, :], 1.0).then_inc(ones_ready, 1)
            dve.wait_ge(ident_one, 1)
            nc.vector.tensor_copy(ident16[:, :], ident[:, :]).then_inc(ident_ready, 1)

            def stats_x(b):
                dve.wait_ge(x_in[load_of[b]], 16)
                nc.vector.bn_stats(stats1[:, b, :], x_sb[:, b, :]).then_inc(stats1_done, 1)
                dve.wait_ge(stats1_done, b + 1)
                nc.vector.bn_aggr(mv1[:, b, :], stats1[:, b, :]).then_inc(mv1_done, 1)

            def q_of(b):
                dve.wait_ge(rstd1_done, b + 1)
                nc.vector.tensor_scalar(q_sb[:, b, :], x_sb[:, b, :], mv1[:, b, 0:1], rstd1[:, b:b + 1],
                                        ALU.subtract, ALU.mult).then_inc(q_vector, 1)

            def residual1(b):
                dve.wait_ge(pv_done, b + 1)
                dve.wait_ge(tg_done, 1)
                nc.vector.scalar_tensor_tensor(out=x1[:, b, :], in0=pv_ps[b % 2][:, 0:N], scalar=tg[:, 0:1],
                                               in1=x_sb[:, b, :], op0=ALU.mult, op1=ALU.add).then_inc(x1_done, 1)

            def stats_x1(b):
                dve.wait_ge(x1_done, b + 1)
                nc.vector.bn_stats(stats2[:, b, :], x1[:, b, :]).then_inc(stats2_done, 1)

            def moments_x1(b):
                dve.wait_ge(stats2_done, b + 1)
                nc.vector.bn_aggr(mv2[:, b, :], stats2[:, b, :]).then_inc(mv2_done, 1)

            def z_of(b):
                dve.wait_ge(rstd2_done, b + 1)
                nc.vector.tensor_scalar(z_sb[:, b, :], x1[:, b, :], mv2[:, b, 0:1], rstd2[:, b:b + 1],
                                        ALU.subtract, ALU.mult).then_inc(z_vector, 1)

            def z_lo(k):
                dve.wait_ge(zhi_done, k + 1)
                tokens = slice(2 * k * P, (2 * k + 2) * P)
                nc.vector.tensor_tensor(
                    zT_lo[:, :, tokens].rearrange("p c (b t) -> p b c t", b=2),
                    z_ps[k][:, :].rearrange("p (b c t) -> p b c t", b=2, c=NC),
                    zT_hi[:, :, tokens].bitcast(F32).rearrange("p c (b t) -> p b c t", b=2),
                    ALU.subtract).then_inc(zlo_done, 1)

            def threshold(i):
                dve.wait_ge(mean_done, i + 1)
                nc.vector.tensor_reduce(sum_abs[:, i:i + 1], mean_ps[:, 0:2], mybir.AxisListType.X,
                                        ALU.add).then_inc(sum_done, 1)
                dve.wait_ge(sum_done, i + 1)
                nc.vector.tensor_scalar(thr[:, i:i + 1], sum_abs[:, i:i + 1], HALF_MEAN, 0.5 * QUANT_EPS,
                                        ALU.mult, ALU.max).then_inc(thr_done, 1)

            def mask(i, h):
                part = slice(h * WCOLS // 2, (h + 1) * WCOLS // 2)
                dve.wait_ge(thr_done, i + 1)
                if i == 1:
                    dve.wait_ge(tern1_done, h + 1)
                nc.vector.tensor_scalar(large[:, part], abs_flat[i][:, part], thr[:, i:i + 1], None,
                                        ALU.is_gt).then_inc(large_done, 1)

            def ternary1(h):
                part = slice(h * WCOLS // 2, (h + 1) * WCOLS // 2)
                dve.wait_ge(large_done, h + 1)
                dve.wait_ge(sign_done, h + 1)
                nc.vector.tensor_tensor(t1_flat[:, part], large[:, part], w_sign[:, 0, part],
                                        ALU.mult).then_inc(tern1_done, 1)

            def ternary2(h):
                part = slice(h * WCOLS // 2, (h + 1) * WCOLS // 2)
                dve.wait_ge(large_done, 3 + h)
                dve.wait_ge(sign_done, 3 + h)
                nc.vector.tensor_tensor(t2_flat[:, part], large[:, part], w_sign[:, 1, part],
                                        ALU.mult).then_inc(tern2_vector, 1)

            def act_copy(u):
                dve.wait_ge(act_done, u + 1)
                nc.vector.tensor_copy(act_hi[:, u, :], act[:, u % GR, :]).then_inc(hi_vector, 1)

            def act_rest(u):
                if u in HI_ON_VECTOR:
                    dve.wait_ge(hi_vector, HI_ON_VECTOR.index(u) + 1)
                else:
                    dve.wait_ge(hi_scalar, hi_count[u])
                nc.vector.tensor_tensor(act_lo[:, u, :], act[:, u % GR, :], act_hi[:, u, :].bitcast(F32),
                                        ALU.subtract).then_inc(lo_done, 1)

            def residual2(b):
                dve.wait_ge(o_done, b + 1)
                dve.wait_ge(x1b_done, b + 1)
                nc.vector.scalar_tensor_tensor(out=out_sb[:, b, :], in0=o_ps[b % 2][:, 0:N], scalar=tg[:, 1:2],
                                               in1=x1b[:, b, :], op0=ALU.mult, op1=ALU.add).then_inc(out_done, 1)

            stats_x(0)
            stats_x(1)
            q_of(0)
            stats_x(2)
            q_of(1)
            stats_x(3)
            q_of(2)
            stats_x(4)
            q_of(3)
            stats_x(5)

            for b in range(B):
                if b == 1:
                    stats_x(6)
                    stats_x(7)
                if b == 2:
                    threshold(0)
                    mask(0, 0)
                if b == 3:
                    mask(0, 1)
                    ternary1(0)
                if b == 4:
                    ternary1(1)
                if b == 6:
                    threshold(1)
                residual1(b)
                stats_x1(b)
                if b == 5:
                    z_lo(0)
                if b == 6:
                    mask(1, 0)
                moments_x1(b)
            z_lo(1)
            mask(1, 1)
            for b in range(Z_ON_POOL, B):
                z_of(b)
            for u in range(0, FIRST_OF_LAST, 2):
                act_copy(u)
                if u == 0:
                    ternary2(1)
                act_copy(u + 1)
                act_rest(u)
                act_rest(u + 1)
                if u == 0:
                    z_lo(2)
                if u == 2:
                    z_lo(3)
            residual2(0)
            for u in range(FIRST_OF_LAST, NU):
                if u in HI_ON_VECTOR:
                    act_copy(u)
                act_rest(u)
                if u == 12:
                    residual2(1)
            for b in range(2, B):
                residual2(b)

        @block.tensor
        def _(pe):
            def ctx_transposes(b):
                pe.wait_ge(c_in[load_of[b]], 16)
                if b >= 2:
                    pe.wait_ge(ctxT_done, b - 1)
                for c in range(NC):
                    mm = nc.tensor.transpose(tr_ps[b % 2][:, c * P:(c + 1) * P], c_sb[:, b, c * P:(c + 1) * P],
                                             ident[:, :])
                mm.then_inc(ctx_tr, 1)

            def scores(b):
                if b < Q_ON_POOL:
                    pe.wait_ge(q_vector, b + 1)
                else:
                    pe.wait_ge(q_pool, b + 1 - Q_ON_POOL)
                if b >= 2:
                    pe.wait_ge(probs_done, b - 1)
                for c in range(NC):
                    mm = nc.tensor.matmul(score_ps[b % 2][:, c * N:(c + 1) * N], q_sb[:, b, c * P:(c + 1) * P],
                                          c_sb[:, b, :], start=True, stop=True)
                mm.then_inc(scores_done, 1)

            def pv(b):
                pe.wait_ge(ctxT_done, b + 1)
                pe.wait_ge(probs_done, b + 1)
                if b >= 2:
                    pe.wait_ge(x1_done, b - 1)
                for c in range(NC):
                    mm = nc.tensor.matmul(pv_ps[b % 2][:, 0:N], ctxT[:, b, c, :], probs[:, b % PR, c, :],
                                          start=(c == 0), stop=(c == NC - 1))
                mm.then_inc(pv_done, 1)

            def z_transposes(k):
                if 2 * k < Z_ON_POOL:
                    pe.wait_ge(z_pool, 2 * k + 2)
                else:
                    pe.wait_ge(z_vector, 2 * k + 2 - Z_ON_POOL)
                if k == 1:
                    pe.wait_ge(thr_done, 2)
                if k >= 2:
                    pe.wait_ge(zlo_done, k - 1)
                for b in range(2):
                    for c in range(NC):
                        mm = nc.tensor.transpose(z_ps[k][:, (2 * b + c) * P:(2 * b + c + 1) * P],
                                                 z_sb[:, 2 * k + b, c * P:(c + 1) * P], ident[:, :])
                mm.then_inc(z_tr, 1)

            def mean(i):
                pe.wait_ge(abs_done, 2 * i + 2)
                pe.wait_ge(ones_ready, 1)
                if i == 1:
                    pe.wait_ge(thr_done, 1)
                mm = nc.tensor.matmul(mean_ps[:, 0:2], ones[:, :], row_abs[:, i, :], start=True, stop=True)
                mm.then_inc(mean_done, 1)

            def w1_transposes(h):
                pe.wait_ge(tern1_done, h + 1)
                pe.wait_ge(ctxT_done, B - 1 + h)
                for j in range(HALF_W):
                    for c in range(NC):
                        mm = nc.tensor.transpose(wt_ps[h][:, :].bitcast(BF16)[:, (j * NC + c) * P:(j * NC + c + 1) * P],
                                                 t1[:, h * HALF_W + j, c * P:(c + 1) * P], ident16[:, :])
                mm.then_inc(w_tr, 1)

            def w2_transposes(h):
                pe.wait_ge(tern2_pool, 1)
                pe.wait_ge(tern2_vector, 1)
                pe.wait_ge(wT_done, 2 - h)
                by_slot = t2[:, :, :].rearrange("p c (f j) -> p c j f", j=FC)
                for j in range(HALF_W):
                    for c in range(NC):
                        mm = nc.tensor.transpose(
                            wt_ps[2 + h][:, :].bitcast(BF16)[:, (j * NC + c) * P:(j * NC + c + 1) * P],
                            by_slot[:, c, h * HALF_W + j, :], ident16[:, :])
                mm.then_inc(w_tr, 1)

            def up(u):
                a, b, slots = units[u]
                n = (b - a) * D
                pe.wait_ge(zlo_done, b // 2)
                pe.wait_ge(wT_done, 1 + slots[-1] // HALF_W)
                if u >= NH:
                    pe.wait_ge(act_done, u - NH + 1)
                    if u - NH not in HI_ON_VECTOR:
                        pe.wait_ge(hi_scalar, hi_count[u - NH])
                elif u < 2:
                    pe.wait_ge(probs_done, B)
                else:
                    pe.wait_ge(x1_done, B + u - 3)
                for i, j in enumerate(slots):
                    for c in range(NC):
                        for k, part in enumerate((zT_hi, zT_lo)):
                            mm = nc.tensor.matmul(h_ps[u % NH][:, i * n:(i + 1) * n], w1T[:, j, c, :],
                                                  part[:, c, a * D:b * D],
                                                  start=(c == 0 and k == 0), stop=(c == NC - 1 and k == 1))
                mm.then_inc(h_done, 1)

            def down(b):
                g = next(i for i, (a, e) in enumerate(GROUPS) if a <= b < e)
                a, e = GROUPS[g]
                n = (e - a) * D
                last = first_unit[g + 1] if g + 1 < len(GROUPS) else NU
                pe.wait_ge(lo_done, last)
                if b == 0:
                    pe.wait_ge(wT_done, 4)
                if b < 2:
                    pe.wait_ge(zlo_done, 3 + b)
                if b >= 2:
                    pe.wait_ge(out_done, b - 1)
                for j in range(FC):
                    u, i = divmod(j * n, UNIT)
                    at = i + (b - a) * D
                    for k, part in enumerate((act_hi, act_lo)):
                        mm = nc.tensor.matmul(o_ps[b % 2][:, 0:N], part[:, first_unit[g] + u, at:at + D], w2T[:, j, :],
                                              start=(j == 0 and k == 0), stop=(j == FC - 1 and k == 1))
                mm.then_inc(o_done, 1)

            pe.wait_ge(warm_zero, 1)
            for _ in range(WARM_UPS):
                nc.tensor.matmul(o_ps[1][:, :], warm[:, 0:P], warm[:, :], start=True, stop=True)
            pe.wait_ge(ident_one, 1)
            ctx_transposes(0)
            for s in range(B):
                if s + 1 < B:
                    ctx_transposes(s + 1)
                scores(s)
                if s >= 2:
                    pv(s - 2)
                if s == 4:
                    mean(0)
                if s == 6:
                    z_transposes(0)
            pe.wait_ge(ident_ready, 1)
            w1_transposes(0)
            mean(1)
            pv(B - 2)
            w1_transposes(1)
            pv(B - 1)
            z_transposes(1)
            for u in range(4):
                up(u)
            z_transposes(2)
            z_transposes(3)
            up(4)
            w2_transposes(0)
            w2_transposes(1)
            up(5)
            up(6)
            up(7)
            down(0)
            for u in range(8, 12):
                up(u)
            down(1)
            for u in range(12, NU):
                up(u)
            for b in range(2, B):
                down(b)


_INS = ["x", "ctx_2048", "g_xattn", "g_ffn", "L0_ffn_w1", "L0_ffn_b1", "L0_ffn_w2", "L0_ffn_b2"]


def kernel(**inputs):
    import numpy as np
    import concourse.bacc as bacc
    from concourse.bass_utils import run_bass_kernel_spmd

    nc = bacc.Bacc("TRN2", target_bir_lowering=False, num_devices=1)
    arrays, args = {}, []
    for name in _INS:
        a = np.ascontiguousarray(inputs[name])
        arrays[f"in_{name}"] = a
        args.append(nc.dram_tensor(f"in_{name}", a.shape, mybir.dt.from_np(a.dtype), kind="ExternalInput").ap())
    shape = inputs["x"].shape
    args.append(nc.dram_tensor("out_x", shape, F32, kind="ExternalOutput").ap())
    flamingo_gated_block(nc, *args)
    r = run_bass_kernel_spmd(nc, [arrays], core_ids=[0])
    return r.results[0]["out_x"]
```
